# Optimizing a Trainium2 kernel written in Bass

```python
import numpy as np
import jax
import jax.numpy as jnp

def _softmax(x, axis=-1):
    return jax.nn.softmax(x, axis=axis)
def _gelu(x):
    return jax.nn.gelu(x, approximate=True)
def _silu(x):
    return jax.nn.silu(x)
def _sigmoid(x):
    return jax.nn.sigmoid(x)
def _layernorm(x, axis=-1, eps=1e-5):
    m = jnp.mean(x, axis=axis, keepdims=True)
    v = jnp.var(x, axis=axis, keepdims=True)
    return (x - m) / jnp.sqrt(v + eps)
def _scatter_add(tgt, idx, src, axis=0):
    return tgt.at[idx].add(src)
def _segment_sum(src, seg, n):
    return jax.ops.segment_sum(src, seg, n)

kernel_name = 'mk_adj_preln_d4_adj_256_368ead'

def setup_inputs(seed: int = 0):
    np.random.seed(seed)
    _w = jnp.asarray
    def _rec_inputs():
        import jax
        import jax.numpy as jnp
        _gk = jax.random.key(seed)
        x = -0.0002928 + 1 * jax.random.normal(jax.random.fold_in(_gk, 1), (32, 512, 256), jnp.float32)
        _a = jax.random.bernoulli(jax.random.fold_in(_gk, 2), 0.0625, (512, 512))
        adj = _a.astype(jnp.int32)
        return x, adj
    x, adj = _rec_inputs()
    def _L0_gnn_setup():
        import jax, jax.numpy as jnp
        import numpy as np
        ALPHA = 0.2
        NEG_INF = -1000000000000.0
        key = jax.random.key(seed)
        k1, k2, k3, k4, k5 = jax.random.split(key, 5)
        B, N, C_in, C_out = (8, 2048, 256, 256)
        inp = jax.random.normal(k1, (B, N, C_in), dtype=jnp.float32)
        adj = jax.random.randint(k2, (N, N), 0, 2, dtype=jnp.int32)
        limit = 1.414 * np.sqrt(6.0 / (C_in + C_out))
        W1 = jax.random.uniform(k3, (C_in, C_out), jnp.float32, -limit, limit)
        W2 = jax.random.uniform(k4, (C_in, C_out), jnp.float32, -limit, limit)
        W3 = jax.random.uniform(k5, (C_in, C_out), jnp.float32, -limit, limit)
        return {'inp': inp, 'adj': adj, 'W1': W1, 'W2': W2, 'W3': W3}
    _L0_gnn_all = _L0_gnn_setup()
    _L0_gnn_in = {k: v for k, v in _L0_gnn_all.items() if k in ('W1', 'W2', 'W3', )}
    del _L0_gnn_all

    def _L1_gnn_setup():
        import jax, jax.numpy as jnp
        import numpy as np
        IN_DIM = 256
        OUT_DIM = 64
        NUM_HEADS = 4
        ALPHA = 0.2
        NEG_INF = -9000000000000000.0
        key = jax.random.key(seed)
        k1, k2, k3, k4 = jax.random.split(key, 4)
        B, N = (4, 2048)
        h = jax.random.normal(k1, (B, N, IN_DIM), dtype=jnp.float32)
        adj = jax.random.randint(k2, (N, N), 0, 2, dtype=jnp.int32)
        W = jax.random.normal(k3, (IN_DIM, NUM_HEADS * OUT_DIM), dtype=jnp.float32) * (1.0 / np.sqrt(IN_DIM))
        a = jax.random.normal(k4, (2 * OUT_DIM,), dtype=jnp.float32) * (1.0 / np.sqrt(2 * OUT_DIM))
        return {'h': h, 'adj': adj, 'W': W, 'a': a}
    _L1_gnn_all = _L1_gnn_setup()
    _L1_gnn_in = {k: v for k, v in _L1_gnn_all.items() if k in ('W', 'a', )}
    del _L1_gnn_all

    def _L2_gnn_setup():
        import jax, jax.numpy as jnp
        import numpy as np
        IN_F = 256
        OUT_F = 256
        N_HEADS = 4
        HEAD_DIM = OUT_F // N_HEADS
        B, N = (8, 2048)
        LN_EPS = 1e-05
        key = jax.random.key(seed)
        ks = jax.random.split(key, 12)
        x = jax.random.normal(ks[0], (B, N, IN_F), dtype=jnp.float32)
        adj = jax.random.randint(ks[1], (N, N), 0, 2, dtype=jnp.int32)
        adj = adj.at[jnp.arange(N), jnp.arange(N)].set(1)
        s = 0.02
        Wq = jax.random.normal(ks[2], (IN_F, OUT_F), jnp.float32) * s
        bq = jnp.zeros((OUT_F,), jnp.float32)
        Wk = jax.random.normal(ks[3], (IN_F, OUT_F), jnp.float32) * s
        bk = jnp.zeros((OUT_F,), jnp.float32)
        Wv = jax.random.normal(ks[4], (IN_F, OUT_F), jnp.float32) * s
        bv = jnp.zeros((OUT_F,), jnp.float32)
        Wo = jax.random.normal(ks[5], (OUT_F, OUT_F), jnp.float32) * s
        bo = jnp.zeros((OUT_F,), jnp.float32)
        gamma = jnp.ones((OUT_F,), jnp.float32)
        beta = jnp.zeros((OUT_F,), jnp.float32)
        return {'x': x, 'adj': adj, 'Wq': Wq, 'bq': bq, 'Wk': Wk, 'bk': bk, 'Wv': Wv, 'bv': bv, 'Wo': Wo, 'bo': bo, 'gamma': gamma, 'beta': beta}
    _L2_gnn_all = _L2_gnn_setup()
    _L2_gnn_in = {k: v for k, v in _L2_gnn_all.items() if k in ('Wq', 'bq', 'Wk', 'bk', 'Wv', 'bv', 'Wo', 'bo', 'gamma', 'beta', )}
    del _L2_gnn_all

    def _L3_gnn_setup():
        import jax, jax.numpy as jnp
        import numpy as np
        ALPHA = 0.2
        MASK_VAL = -9000000000000000.0
        key = jax.random.key(seed)
        k1, k2, k3, k4 = jax.random.split(key, 4)
        B, N, F = (8, 1024, 256)
        H, OUT = (4, 256)
        hs = OUT // H
        x = jax.random.normal(k1, (B, N, F), dtype=jnp.float32)
        adj = jax.random.randint(k2, (N, N), 0, 2, dtype=jnp.int32)
        wb = float(np.sqrt(6.0 / (F + hs)))
        ab = float(np.sqrt(6.0 / (H + 2 * hs)))
        W = jax.random.uniform(k3, (H, F, hs), dtype=jnp.float32, minval=-wb, maxval=wb)
        a = jax.random.uniform(k4, (H, 2 * hs), dtype=jnp.float32, minval=-ab, maxval=ab)
        return {'x': x, 'adj': adj, 'W': W, 'a': a}
    _L3_gnn_all = _L3_gnn_setup()
    _L3_gnn_in = {k: v for k, v in _L3_gnn_all.items() if k in ('W', 'a', )}
    del _L3_gnn_all

    return {
        "x": x,
        "adj": adj,
        "L0_gnn_W1": _L0_gnn_in["W1"],
        "L0_gnn_W2": _L0_gnn_in["W2"],
        "L0_gnn_W3": _L0_gnn_in["W3"],
        "L1_gnn_W": _L1_gnn_in["W"],
        "L1_gnn_a": _L1_gnn_in["a"],
        "L2_gnn_Wq": _L2_gnn_in["Wq"],
        "L2_gnn_bq": _L2_gnn_in["bq"],
        "L2_gnn_Wk": _L2_gnn_in["Wk"],
        "L2_gnn_bk": _L2_gnn_in["bk"],
        "L2_gnn_Wv": _L2_gnn_in["Wv"],
        "L2_gnn_bv": _L2_gnn_in["bv"],
        "L2_gnn_Wo": _L2_gnn_in["Wo"],
        "L2_gnn_bo": _L2_gnn_in["bo"],
        "L2_gnn_gamma": _L2_gnn_in["gamma"],
        "L2_gnn_beta": _L2_gnn_in["beta"],
        "L3_gnn_W": _L3_gnn_in["W"],
        "L3_gnn_a": _L3_gnn_in["a"],
    }

def reference(x, adj, L0_gnn_W1, L0_gnn_W2, L0_gnn_W3, L1_gnn_W, L1_gnn_a, L2_gnn_Wq, L2_gnn_bq, L2_gnn_Wk, L2_gnn_bk, L2_gnn_Wv, L2_gnn_bv, L2_gnn_Wo, L2_gnn_bo, L2_gnn_gamma, L2_gnn_beta, L3_gnn_W, L3_gnn_a):
    import jax
    import jax.numpy as jnp
    def _L0_gnn_ref(inp, adj, W1, W2, W3):
        import jax, jax.numpy as jnp
        import numpy as np
        ALPHA = 0.2
        NEG_INF = -1000000000000.0
        h1 = jnp.einsum('bnc,cd->bnd', inp, W1)
        h2 = jnp.einsum('bnc,cd->bnd', inp, W2)
        h3 = jnp.einsum('bnc,cd->bnd', inp, W3)
        e = jnp.einsum('bnd,bmd->bnm', h1, h2)
        e = jax.nn.leaky_relu(e, ALPHA)
        e = jnp.where(adj[None, :, :] > 0, e, NEG_INF)
        attention = jax.nn.softmax(e, axis=-1)
        h_prime = jnp.einsum('bnm,bmd->bnd', attention, h3)
        return jax.nn.relu(h_prime)

    def _L1_gnn_ref(h, adj, W, a):
        import jax, jax.numpy as jnp
        import numpy as np
        IN_DIM = 256
        OUT_DIM = 64
        NUM_HEADS = 4
        ALPHA = 0.2
        NEG_INF = -9000000000000000.0
        B, N, _ = h.shape
        H, D = (NUM_HEADS, OUT_DIM)
        q = (h @ W).reshape(B, N, H, D)
        a_src, a_dst = (a[:D], a[D:])
        e_src = jnp.einsum('bnhd,d->bnh', q, a_src)
        e_dst = jnp.einsum('bnhd,d->bnh', q, a_dst)
        e = e_src[:, :, None, :] + e_dst[:, None, :, :]
        e = jnp.where(e >= 0, e, ALPHA * e)
        mask = (adj > 0)[None, :, :, None]
        e = jnp.where(mask, e, NEG_INF)
        attn = jax.nn.softmax(e, axis=2)
        h_prime = jnp.einsum('bijh,bjhd->bihd', attn, q)
        return jax.nn.elu(h_prime.reshape(B, N, H * D))

    def _L2_gnn_ref(x, adj, Wq, bq, Wk, bk, Wv, bv, Wo, bo, gamma, beta):
        import jax, jax.numpy as jnp
        import numpy as np
        IN_F = 256
        OUT_F = 256
        N_HEADS = 4
        HEAD_DIM = OUT_F // N_HEADS
        B, N = (8, 2048)
        LN_EPS = 1e-05
        b, n, _ = x.shape
        Q = (x @ Wq + bq).reshape(b, n, N_HEADS, HEAD_DIM)
        K = (x @ Wk + bk).reshape(b, n, N_HEADS, HEAD_DIM)
        V = (x @ Wv + bv).reshape(b, n, N_HEADS, HEAD_DIM)
        scale = 1.0 / np.sqrt(HEAD_DIM).astype(np.float32)
        scores = jnp.einsum('bnhd,bmhd->bhnm', Q, K) * scale
        mask = (adj == 0)[None, None, :, :]
        scores = jnp.where(mask, -jnp.inf, scores)
        attn = jax.nn.softmax(scores, axis=-1)
        out = jnp.einsum('bhnm,bmhd->bnhd', attn, V).reshape(b, n, OUT_F)
        out = out @ Wo + bo
        mu = jnp.mean(out, axis=-1, keepdims=True)
        var = jnp.mean(jnp.square(out - mu), axis=-1, keepdims=True)
        out = (out - mu) / jnp.sqrt(var + LN_EPS) * gamma + beta
        return out

    def _L3_gnn_ref(x, adj, W, a):
        import jax, jax.numpy as jnp
        import numpy as np
        ALPHA = 0.2
        MASK_VAL = -9000000000000000.0
        B, N, _ = x.shape
        H, _, hs = W.shape
        Wh = jnp.einsum('bnf,hfd->bhnd', x, W)
        a1, a2 = (a[:, :hs], a[:, hs:])
        ei = jnp.einsum('bhnd,hd->bhn', Wh, a1)
        ej = jnp.einsum('bhnd,hd->bhn', Wh, a2)
        e = ei[:, :, :, None] + ej[:, :, None, :]
        e = jnp.where(e > 0, e, ALPHA * e)
        e = jnp.where(adj[None, None] > 0, e, MASK_VAL)
        att = jax.nn.softmax(e, axis=-1)
        h = jnp.einsum('bhij,bhjd->bhid', att, Wh)
        h = h.transpose(0, 2, 1, 3).reshape(B, N, H * hs)
        return jax.nn.elu(h)

    h = jnp.maximum(_layernorm(x, axis=-1), 0.0)
    x = x + _L0_gnn_ref(h, adj, L0_gnn_W1, L0_gnn_W2, L0_gnn_W3)
    h = jnp.maximum(_layernorm(x, axis=-1), 0.0)
    x = x + _L1_gnn_ref(h, adj, L1_gnn_W, L1_gnn_a)
    h = jnp.maximum(_layernorm(x, axis=-1), 0.0)
    x = x + _L2_gnn_ref(h, adj, L2_gnn_Wq, L2_gnn_bq, L2_gnn_Wk, L2_gnn_bk, L2_gnn_Wv, L2_gnn_bv, L2_gnn_Wo, L2_gnn_bo, L2_gnn_gamma, L2_gnn_beta)
    h = jnp.maximum(_layernorm(x, axis=-1), 0.0)
    x = x + _L3_gnn_ref(h, adj, L3_gnn_W, L3_gnn_a)
    return x


_drawn_inputs = setup_inputs


def setup_inputs(seed=0):
    import zlib

    import numpy as np

    out = dict(_drawn_inputs(seed))
    spreads = {'L2_gnn_bq': (0.0, 0.8),
     'L2_gnn_bk': (0.0, 0.8),
     'L2_gnn_bv': (0.0, 0.1),
     'L2_gnn_bo': (0.0, 0.1),
     'L2_gnn_gamma': (1.0, 0.2),
     'L2_gnn_beta': (0.0, 0.1)}
    factors = {'L1_gnn_a': 2.977, 'L2_gnn_Wq': 8.0, 'L2_gnn_Wk': 8.0}
    for name, (base, spread) in spreads.items():
        noise = np.random.default_rng([zlib.crc32(name.encode()), seed]).standard_normal(out[name].shape)
        drawn = base * np.exp(spread * noise) if base else spread * noise
        out[name] = jnp.asarray(drawn.astype(out[name].dtype))
    for name, factor in factors.items():
        out[name] = (out[name] * factor).astype(out[name].dtype)
    return out
```

```python
import concourse.bass as bass
from concourse import mybir
from contextlib import ExitStack


def gnn_stack_kernel(nc, x, adj, W1, W2, W3, gat1_W, gat1_a, Wq, bq, Wk, bk, Wv, bv, Wo, bo,
                     gamma, beta, gat3_W, gat3_a, out):
    f32 = mybir.dt.float32
    i32 = mybir.dt.int32
    ALU = mybir.AluOpType
    ACT = mybir.ActivationFunctionType
    AX = mybir.AxisListType

    P = 128
    B, N, C = x.shape
    NT = N // P
    KT = C // P
    H = gat3_W.shape[0]
    D = C // H
    QE = C + 2 * H
    DV = D + 1
    ST = 2
    STEPS = B // ST
    EPS = 1e-5
    SLOPE = 0.2
    MASKED = -1e30
    LOWEST = -3e38
    QK_SCALE = float(D) ** -0.5
    GAT = {1: 0, 3: 1}
    NORMS = {0: 0, 1: 1, 2: 2, "inner": 3, 3: 4}
    streams = range(ST)

    ctx = ExitStack()
    with ctx:
        def sb(name, shape, dt=f32):
            return ctx.enter_context(nc.sbuf_tensor(name, shape, dt))

        ident = sb("ident", [P, P])
        minus_half = sb("minus_half", [P, NT])
        adjT = sb("adjT", [P, NT, N])
        mask_pos = sb("mask_pos", [P, NT, N])
        mask_nz = sb("mask_nz", [P, NT, N])
        wA = sb("wA", [P, KT, C])
        w3 = sb("w3", [P, KT, C])
        wgat = sb("wgat", [P, 2, KT, QE])
        a_bc = sb("a_bc", [P, 2, H, 2 * D])
        wqkvo = sb("wqkvo", [P, 4, KT, C])
        b_qk = sb("b_qk", [P, 2, KT])
        b_rows = sb("b_rows", [P, 4, C])

        def per_stream(name, shape):
            return [sb(f"{name}{s}", shape) for s in streams]

        x_in = per_stream("x_in", [P, NT, C])
        xc = per_stream("xc", [P, NT, C])
        x_out = per_stream("x_out", [P, NT, C])
        stats = per_stream("stats", [P, NT, 6])
        mv = per_stream("mv", [P, NT, 2])
        rstd = per_stream("rstd", [P, NT])
        hn = per_stream("hn", [P, NT, C])
        hT = per_stream("hT", [P, KT, N])
        qT = per_stream("qT", [P, KT, N])
        kT = per_stream("kT", [P, KT, N])
        vals = per_stream("vals", [P, NT, H * DV])
        qx = per_stream("qx", [P, NT, QE])
        prob = per_stream("prob", [P, 2, NT, N])
        probT = per_stream("probT", [P, 2, NT, N])
        rowmax = per_stream("rowmax", [P, H, NT])
        negmax = per_stream("negmax", [P, H, NT])
        rowsum = per_stream("rowsum", [P, H, NT])
        rinv = per_stream("rinv", [P, H, NT])
        dmax = per_stream("dmax", [H, 1])
        gexp = per_stream("gexp", [P, 3, NT, H])
        gval = per_stream("gval", [P, 3, NT, H])

        adj_i = probT[0][:, 0, :, :].bitcast(i32)
        adj_pos = probT[0][:, 1, :, :]
        w12 = probT[1][:, 0, 0:2, :].rearrange("p a (k c) -> p a k c", k=KT)
        w12T = probT[1][:, 0, 2:4, :].rearrange("p a (k c) -> p a k c", k=KT)
        wa_tmp = probT[1][:, 1, 0:2, :].rearrange("p a (k h d) -> p a k h d", k=KT, h=H)

        row_any = sb("row_any", [P, NT])
        part_any = sb("part_any", [P, 1])
        all_any = sb("all_any", [1, 1])
        minus_one = sb("minus_one", [P, 1])

        ps = [ctx.enter_context(nc.psum_tensor(f"ps{s}", [P, 4, 512], f32)) for s in streams]

        def sem(name):
            return ctx.enter_context(nc.semaphore(name))

        consts_in = sem("consts_in")
        bias_in = sem("bias_in")
        ident_ok = sem("ident_ok")
        masks_ok = sem("masks_ok")
        setup_pe = sem("setup_pe")
        setup_ok = sem("setup_ok")
        wa_ok = sem("wa_ok")
        poison_ok = sem("poison_ok")

        dve_waits = sem("dve_waits")
        pe_waits = sem("pe_waits")
        pool_waits = sem("pool_waits")

        class Signal:

            def __init__(self, name, per_step):
                self.name, self.per_step = name, per_step
                self.sems = [sem(f"{name}{s}") for s in streams]

            def wait(self, eng, s, i, n):
                eng.wait_ge(self.sems[s], i * self.per_step + n)

            def wait_apart(self, eng, s, i, n, waits_done):
                self.wait(eng, s, i, n)
                eng.sem_inc(waits_done, 1)

            def __getitem__(self, s):
                return self.sems[s]

        x_loaded = Signal("x_loaded", 16)
        x_stored = Signal("x_stored", 16)
        out_free = Signal("out_free", 1)
        out_ready = Signal("out_ready", 1)
        x_ready = Signal("x_ready", 1)
        x1_ready = Signal("x1_ready", 1)
        x2_ready = Signal("x2_ready", 1)
        stats_ok = Signal("stats_ok", 5)
        mv_ready = Signal("mv_ready", 5)
        var_eps = Signal("var_eps", 5)
        rstd_ready = Signal("rstd_ready", 5)
        hn_ready = Signal("hn_ready", 4)
        hTp_ready = Signal("hTp_ready", 4)
        hT_ready = Signal("hT_ready", 4)
        uTp_ready = Signal("uTp_ready", 1)
        uT_ready = Signal("uT_ready", 1)
        valp_ready = Signal("valp_ready", 2)
        val_ready = Signal("val_ready", 2)
        e_ready = Signal("e_ready", NT + H * NT)
        masked = Signal("masked", NT + H * NT)
        shift_a = Signal("shift_a", 1)
        shift_ready = Signal("shift_ready", 1 + H)
        lrelu_ready = Signal("lrelu_ready", NT)
        p_ready = Signal("p_ready", NT + H * NT)
        pTp_ready = Signal("pTp_ready", NT + H * NT)
        pT_act = Signal("pT_act", (NT + H * NT) // 2)
        pT_dve = Signal("pT_dve", (NT + H * NT) // 2)
        agg0_ready = Signal("agg0_ready", 1)
        rinv0 = Signal("rinv0", 1)
        agg0_norm = Signal("agg0_norm", 1)
        q_ready = Signal("q_ready", 2)
        qx_ready = Signal("qx_ready", 2)
        dT_ready = Signal("dT_ready", 2)
        dmax_ready = Signal("dmax_ready", 2)
        dmax_bc = Signal("dmax_bc", 2)
        delta_a = Signal("delta_a", 2)
        gexp_ready = Signal("gexp_ready", 2)
        gval_ready = Signal("gval_ready", 2)
        gvals_ready = Signal("gvals_ready", 2)
        r_ready = Signal("r_ready", 2 * H)
        gP_ready = Signal("gP_ready", 2 * H)
        gagg_ready = Signal("gagg_ready", 2 * H)
        grinv = Signal("grinv", 2 * H)
        gnorm = Signal("gnorm", 2 * H)
        zmin_ready = Signal("zmin_ready", 2)
        elu_e = Signal("elu_e", 2)
        elu_r = Signal("elu_r", 2)
        xr_ready = Signal("xr_ready", 2)
        qkp_ready = Signal("qkp_ready", 1)
        qT_ready = Signal("qT_ready", 1)
        kT_ready = Signal("kT_ready", 1)
        agg2_ready = Signal("agg2_ready", H)
        rinv2 = Signal("rinv2", H)
        agg2_norm = Signal("agg2_norm", H)
        oTp_ready = Signal("oTp_ready", 1)
        oT_ready = Signal("oT_ready", 1)
        wop_ready = Signal("wop_ready", 1)
        o_ready = Signal("o_ready", 1)
        on_ready = Signal("on_ready", 1)
        xb_ready = Signal("xb_ready", 1)

        x_dram = x.rearrange("(i s) (t p) c -> i s p t c", s=ST, p=P)
        out_dram = out.rearrange("(i s) (t p) c -> i s p t c", s=ST, p=P)

        def rows(ap):
            return ap.rearrange("(t p) n -> p t n", p=P)

        CONST_DMAS = [
            (adj_i[:, :, :], rows(adj)),
            (w12[:, 0, :, :], rows(W1)), (w12[:, 1, :, :], rows(W2)), (w3[:, :, :], rows(W3)),
            (wgat[:, 0, :, 0:C], rows(gat1_W)),
            *[(wgat[:, 1, k, 0:C].rearrange("p (h d) -> p h d", h=H),
               gat3_W[:, k * P:(k + 1) * P, :].rearrange("h p d -> p h d")) for k in range(KT)],
            *[(wqkvo[:, n, :, :], rows(w)) for n, w in enumerate((Wq, Wk, Wv, Wo))],
        ]
        BIAS_DMAS = [
            *[(b_qk[:, n, :], b.rearrange("(t p) -> p t", p=P)) for n, b in enumerate((bq, bk))],
            *[(b_rows[:, n, :], b.rearrange("(o c) -> o c", o=1).broadcast_to([P, C]))
              for n, b in enumerate((bv, bo, gamma, beta))],
            *[(a_bc[:, 0, h, :], gat1_a.rearrange("(o c) -> o c", o=1).broadcast_to([P, 2 * D]))
              for h in range(H)],
            *[(a_bc[:, 1, h, :], gat3_a[h:h + 1, :].broadcast_to([P, 2 * D])) for h in range(H)],
        ]
        CONSTS = 16 * len(CONST_DMAS)
        BIASES = 16 * len(BIAS_DMAS)

        def two_banks(s, first):
            return ps[s][:, first:first + 2, :].rearrange("p b (t c) -> p (b t) c", c=C)

        def att(layer, h, t):
            return t if layer == 0 else NT + h * NT + t

        block = ctx.enter_context(nc.Block())

        @block.sync
        def _(sp):
            for dst, src in CONST_DMAS:
                sp.dma_start(dst, src).then_inc(consts_in, 16)
            for s in streams:
                sp.sem_inc(out_free[s], 1)
                sp.dma_start(x_in[s][:, :, :], x_dram[0, s]).then_inc(x_loaded[s], 16)
            with sp.Fori(1, STEPS) as i:
                before = sp.snap(i - 1)
                taken = sp.snap((i - 1) * x_ready.per_step + 1)
                stored = sp.snap(i * 16)
                for s in streams:
                    sp.wait_ge(x_ready[s], taken)
                    sp.dma_start(x_in[s][:, :, :], x_dram[i, s]).then_inc(x_loaded[s], 16)
                for s in streams:
                    sp.wait_ge(out_ready[s], i)
                    sp.dma_start(out_dram[before, s], x_out[s][:, :, :]).then_inc(x_stored[s], 16)
                for s in streams:
                    sp.wait_ge(x_stored[s], stored)
                    sp.sem_inc(out_free[s], 1)
            for s in streams:
                sp.wait_ge(out_ready[s], STEPS)
                sp.dma_start(out_dram[STEPS - 1, s], x_out[s][:, :, :]).then_inc(x_stored[s], 16)
            for s in streams:
                sp.wait_ge(x_stored[s], 16 * STEPS)

        @block.gpsimd
        def _(pool):
            nc.gpsimd.memset(ident[:, :], 0.0).then_inc(ident_ok, 1)
            nc.gpsimd.memset(minus_half[:, :], -0.5).then_inc(ident_ok, 1)
            for dst, src in BIAS_DMAS:
                pool.dma_start(dst, src, allow_slow_non_contiguous=True).then_inc(bias_in, 16)
            pool.wait_ge(ident_ok, 2)
            nc.gpsimd.affine_select(out=ident[:, :], in_=ident[:, :], compare_op=ALU.not_equal,
                                    fill=1.0, base=0, pattern=[[-1, P]],
                                    channel_multiplier=1).then_inc(ident_ok, 1)

            def deviation(i, s, norm):
                n = NORMS[norm]
                mv_ready.wait_apart(pool, s, i, n + 1, pool_waits)
                nc.gpsimd.tensor_scalar(rstd[s][:, :], mv[s][:, :, 1], EPS, None,
                                        ALU.add).then_inc(var_eps[s], 1)
                var_eps.wait(pool, s, i, n + 1)
                nc.gpsimd.tensor_tensor(rstd[s][:, :], rstd[s][:, :], minus_half[:, :],
                                        ALU.pow).then_inc(rstd_ready[s], 1)

            def gat_values(i, s, layer):
                g = GAT[layer]
                gval_ready.wait(pool, s, i, g + 1)
                out = vals[s][:, :, :].rearrange("p t (h e) -> p t h e", h=H)
                for t in range(NT):
                    v = gval[s][:, 0, t, :].unsqueeze(2).broadcast_to([P, H, D])
                    nc.gpsimd.tensor_tensor(
                        out[:, t, :, 0:D], qx[s][:, t, 0:C].rearrange("p (h d) -> p h d", h=H), v,
                        ALU.mult)
                nc.gpsimd.tensor_copy(out[:, :, :, D], gval[s][:, 0, :, :]).then_inc(gvals_ready[s], 1)

            def gat_residual(i, s, layer):
                g = GAT[layer]
                elu_r.wait(pool, s, i, g + 1)
                nc.gpsimd.tensor_tensor(prob[s][:, 0, :, 0:C], prob[s][:, 0, :, 0:C], xc[s][:, :, :],
                                        ALU.add).then_inc(xr_ready[s], 1)

            pool.wait_ge(ident_ok, 3)
            with pool.Fori(0, STEPS) as i:
                for s in streams:
                    deviation(i, s, 0)
                for s in streams:
                    agg0_norm.wait(pool, s, i, 1)
                    nc.gpsimd.tensor_tensor(xc[s][:, :, :], x_in[s][:, :, :], hn[s][:, :, :],
                                            ALU.add).then_inc(x_ready[s], 1)
                for layer in (1, 3):
                    for s in streams:
                        deviation(i, s, layer)
                    for s in streams:
                        gat_values(i, s, layer)
                    for s in streams:
                        gat_residual(i, s, layer)
                    if layer == 3:
                        break
                    for s in streams:
                        deviation(i, s, 2)
                    for s in streams:
                        hn_ready.wait(pool, s, i, 3)
                        nc.gpsimd.tensor_tensor(
                            xc[s][:, :, :], xc[s][:, :, :],
                            b_rows[:, 3, :].unsqueeze(1).broadcast_to([P, NT, C]),
                            ALU.add).then_inc(xb_ready[s], 1)
                    for s in streams:
                        deviation(i, s, "inner")

        @block.scalar
        def _(act):
            def h_transposed(i, s, layer):
                hTp_ready.wait(act, s, i, layer + 1)
                nc.scalar.activation(hT[s][:, :, :], ps[s][:, 0:2, :], ACT.Relu).then_inc(hT_ready[s], 1)

            def exponentials(i, s, layer, h, t):
                a = att(layer, h, t)
                buf = h % 2
                scale = 1.0 if layer == 0 else QK_SCALE
                if layer == 0:
                    lrelu_ready.wait(act, s, i, t + 1)
                if t == 0:
                    shift_ready.wait(act, s, i, 1 if layer == 0 else h + 2)
                nc.scalar.activation(prob[s][:, buf, t, :], prob[s][:, buf, t, :], ACT.Exp,
                                     bias=negmax[s][:, h, t:t + 1], scale=scale,
                                     accum_out=rowsum[s][:, h, t:t + 1]).then_inc(p_ready[s], 1)

            def weights_out(i, s, layer, h, t):
                a = att(layer, h, t)
                bank = (2 + t) % 4 if layer == 0 else 2
                pTp_ready.wait(act, s, i, a + 1)
                nc.scalar.copy(probT[s][:, 0, :, t * P:(t + 1) * P],
                               ps[s][:, bank, :].rearrange("p (j n) -> p j n", j=NT)).then_inc(pT_act[s], 1)

            def gat(i, layer):
                g = GAT[layer]
                for s in streams:
                    q_ready.wait(act, s, i, g + 1)
                    nc.scalar.copy(qx[s][:, :, :], ps[s][:, :, 0:QE]).then_inc(qx_ready[s], 1)
                for s in streams:
                    gexp_ready.wait(act, s, i, g + 1)
                    for n, scale in enumerate((SLOPE, 1 - SLOPE, 1.0)):
                        last = nc.scalar.activation(gval[s][:, n, :, :], gexp[s][:, n, :, :], ACT.Exp,
                                                    scale=scale)
                    last.then_inc(gval_ready[s], 1)
                for s in streams:
                    gnorm.wait(act, s, i, g * H + H)
                    nc.scalar.activation(prob[s][:, 0, :, 0:C], hn[s][:, :, :],
                                         ACT.Relu).then_inc(elu_r[s], 1)
                    zmin_ready.wait(act, s, i, g + 1)
                    nc.scalar.activation(prob[s][:, 1, :, 0:C], prob[s][:, 1, :, 0:C],
                                         ACT.Exp).then_inc(elu_e[s], 1)

            act.wait_ge(bias_in, BIASES)
            with act.Fori(0, STEPS) as i:
                for s in streams:
                    h_transposed(i, s, 0)
                for s in streams:
                    uTp_ready.wait(act, s, i, 1)
                    nc.scalar.copy(qT[s][:, :, :], ps[s][:, 2:4, :]).then_inc(uT_ready[s], 1)
                for t in range(NT):
                    for s in streams:
                        exponentials(i, s, 0, 0, t)
                for t in range(0, NT, 2):
                    for s in streams:
                        weights_out(i, s, 0, 0, t)
                for s in streams:
                    h_transposed(i, s, 1)
                gat(i, 1)
                for s in streams:
                    h_transposed(i, s, 2)
                for s in streams:
                    qkp_ready.wait(act, s, i, 1)
                    for k in range(KT):
                        last = nc.scalar.activation(qT[s][:, k, :], ps[s][:, k, :], ACT.Identity,
                                                    bias=b_qk[:, 0, k:k + 1])
                    last.then_inc(qT_ready[s], 1)
                for h in range(-1, H):
                    if h >= 0:
                        for t in range(0, NT, 2):
                            for s in streams:
                                weights_out(i, s, 2, h, t)
                    if h + 1 < H:
                        for t in range(NT):
                            for s in streams:
                                exponentials(i, s, 2, h + 1, t)
                for s in streams:
                    oTp_ready.wait(act, s, i, 1)
                    nc.scalar.copy(qT[s][:, :, :], ps[s][:, 0:2, :]).then_inc(oT_ready[s], 1)
                for s in streams:
                    h_transposed(i, s, 3)
                gat(i, 3)

        @block.vector
        def _(dve):
            dve.wait_ge(consts_in, CONSTS)
            nc.vector.tensor_scalar(adj_pos[:, :, :], adj_i[:, :, :], 0, None, ALU.is_gt).then_inc(masks_ok, 1)
            nc.vector.tensor_scalar(mask_pos[:, :, :], adj_i[:, :, :], 0, MASKED, ALU.is_le, ALU.mult)
            nc.vector.tensor_scalar(mask_nz[:, :, :], adj_i[:, :, :], 0, MASKED, ALU.is_equal,
                                    ALU.mult).then_inc(masks_ok, 1)
            dve.wait_ge(bias_in, BIASES)
            n = 0
            for g in range(2):
                for side in range(2):
                    for k in range(KT):
                        if g:
                            dve.wait_ge(wa_ok, n - 4 + 1)
                        nc.vector.tensor_tensor(
                            wa_tmp[:, side, k, :, :],
                            wgat[:, g, k, 0:C].rearrange("p (h d) -> p h d", h=H),
                            a_bc[:, g, :, side * D:(side + 1) * D], ALU.mult).then_inc(wa_ok, 1)
                        n += 1
                        dve.wait_ge(wa_ok, n)
                        nc.vector.reduce_sum(wgat[:, g, k, C + side * H:C + (side + 1) * H],
                                             wa_tmp[:, side, k, :, :], AX.X).then_inc(wa_ok, 1)
                        n += 1
            dve.wait_ge(masks_ok, 2)
            nc.vector.reduce_max(row_any[:, :], mask_nz[:, :, :], AX.X).then_inc(poison_ok, 1)
            dve.wait_ge(poison_ok, 1)
            nc.vector.tensor_reduce(part_any[:, :], row_any[:, :], AX.X, ALU.min).then_inc(poison_ok, 1)
            dve.wait_ge(setup_pe, 1)
            nc.vector.tensor_copy(w12T[:, :, :, :].rearrange("p a k c -> p (a k) c"),
                                  ps[1][:, :, 0:C]).then_inc(setup_ok, 1)
            dve.wait_ge(setup_pe, 2)
            nc.vector.tensor_copy(adjT[:, :, :], ps[0][:, :, :]).then_inc(setup_ok, 1)
            dve.wait_ge(setup_pe, 3)
            nc.vector.tensor_copy(wA[:, :, :], ps[1][:, 0:KT, 0:C]).then_inc(setup_ok, 1)
            dve.wait_ge(setup_pe, 4)
            nc.vector.tensor_reduce(all_any[:, :], ps[0][0:1, 0, 0:P], AX.X, ALU.min).then_inc(setup_ok, 1)
            dve.wait_ge(setup_pe, 5)
            nc.vector.tensor_scalar(minus_one[:, :], ps[0][:, 1, 0:1], 1e30, 0.0, ALU.mult,
                                    ALU.mult).then_inc(poison_ok, 1)
            dve.wait_ge(poison_ok, 3)
            nc.vector.tensor_scalar(minus_one[:, :], minus_one[:, :], -1.0, None,
                                    ALU.add).then_inc(setup_ok, 1)
            dve.wait_ge(setup_ok, 5)

            def statistics(i, s, norm, rows_of):
                n = NORMS[norm]
                for t in range(NT):
                    last = nc.vector.bn_stats(stats[s][:, t, :], rows_of[:, t, :])
                last.then_inc(stats_ok[s], 1)
                stats_ok.wait_apart(dve, s, i, n + 1, dve_waits)
                for t in range(NT):
                    last = nc.vector.bn_aggr(mv[s][:, t, :], stats[s][:, t, :])
                last.then_inc(mv_ready[s], 1)

            def normalised(i, s, norm, rows_of, ready):
                rstd_ready.wait(dve, s, i, NORMS[norm] + 1)
                for t in range(NT):
                    last = nc.vector.tensor_scalar(hn[s][:, t, :], rows_of[:, t, :], mv[s][:, t, 0:1],
                                                   rstd[s][:, t:t + 1], ALU.subtract, ALU.mult)
                last.then_inc(ready[s], 1)

            def layer_statistics(i, s, layer):
                if layer == 0:
                    x_loaded.wait(dve, s, i, 16)
                else:
                    x_wait(i, s, layer)
                statistics(i, s, layer, x_in[s] if layer == 0 else xc[s])

            def norm_layer(i, layer):
                if layer < 2:
                    for s in streams:
                        layer_statistics(i, s, layer)
                for s in streams:
                    normalised(i, s, layer, x_in[s] if layer == 0 else xc[s], hn_ready)

            def x_wait(i, s, layer):
                x_ready_by = {1: (x_ready, 1), 2: (x1_ready, 1), 3: (x2_ready, 1)}
                signal, n = x_ready_by[layer]
                signal.wait(dve, s, i, n)

            def masked_max(i, s, layer, h, t):
                a = att(layer, h, t)
                buf = h % 2
                bank = (2 + t) % 4 if layer == 0 else t % 2
                mask = mask_pos if layer == 0 else mask_nz
                e_ready.wait_apart(dve, s, i, a + 1, dve_waits)
                nc.vector.tensor_tensor_reduce(
                    out=prob[s][:, buf, t, :], in0=ps[s][:, bank, :], in1=mask[:, t, :], scale=1.0,
                    scalar=LOWEST, op0=ALU.add, op1=ALU.max,
                    accum_out=rowmax[s][:, h, t:t + 1]).then_inc(masked[s], 1)

            def weights_out(i, s, layer, h, t):
                a = att(layer, h, t)
                bank = (2 + t) % 4 if layer == 0 else 2
                pTp_ready.wait(dve, s, i, a + 1)
                nc.vector.tensor_copy(probT[s][:, 0, :, t * P:(t + 1) * P],
                                      ps[s][:, bank, :].rearrange("p (j n) -> p j n", j=NT)).then_inc(pT_dve[s], 1)

            def gat(i, layer):
                g = GAT[layer]
                for s in streams:
                    dT_ready.wait(dve, s, i, g + 1)
                    nc.vector.reduce_max(dmax[s][:, :], ps[s][0:H, 0, :], AX.X).then_inc(dmax_ready[s], 1)
                for s in streams:
                    dmax_bc.wait(dve, s, i, g + 1)
                    top = ps[s][:, 1, 0:H].unsqueeze(1).broadcast_to([P, NT, H])
                    nc.vector.tensor_tensor(gexp[s][:, 0, :, :], qx[s][:, :, C + H:QE], top, ALU.subtract)
                    nc.vector.tensor_tensor(gexp[s][:, 1, :, :], qx[s][:, :, C + H:QE], top, ALU.subtract)
                    nc.vector.tensor_tensor(gexp[s][:, 2, :, :], qx[s][:, :, C:C + H], top,
                                            ALU.add).then_inc(delta_a[s], 1)
                for s in streams:
                    delta_a.wait(dve, s, i, g + 1)
                    nc.vector.tensor_scalar(gexp[s][:, 2, :, :], gexp[s][:, 2, :, :], -(1 - SLOPE), 0.0,
                                            ALU.mult, ALU.min).then_inc(gexp_ready[s], 1)
                for h in range(H + 1):
                    for s in streams:
                        if h < H:
                            r_ready.wait(dve, s, i, g * H + h + 1)
                            for t in range(NT):
                                last = nc.vector.scalar_tensor_tensor(
                                    out=probT[s][:, h % 2, t, :], in0=ps[s][:, 2 + h % 2, :],
                                    scalar=gval[s][:, 1, t, h:h + 1], in1=adjT[:, t, :],
                                    op0=ALU.max, op1=ALU.mult)
                            last.then_inc(gP_ready[s], 1)
                        if h:
                            gat_norm(i, s, g, h - 1)
                for s in streams:
                    gnorm.wait(dve, s, i, g * H + H)
                    nc.vector.tensor_scalar(prob[s][:, 1, :, 0:C], hn[s][:, :, :], 0.0, None,
                                            ALU.min).then_inc(zmin_ready[s], 1)
                for s in streams:
                    xr_ready.wait(dve, s, i, g + 1)
                    elu_e.wait(dve, s, i, g + 1)
                    if layer == 3:
                        out_free.wait(dve, s, i, 1)
                    dst, ready = (xc, x1_ready) if layer == 1 else (x_out, out_ready)
                    nc.vector.scalar_tensor_tensor(
                        out=dst[s][:, :, :], in0=prob[s][:, 1, :, 0:C], scalar=minus_one[:, 0:1],
                        in1=prob[s][:, 0, :, 0:C], op0=ALU.add, op1=ALU.add).then_inc(ready[s], 1)
                    if layer == 1:
                        layer_statistics(i, s, 2)

            def gat_norm(i, s, g, h):
                n = g * H + h + 1
                agg = ps[s][:, h % 2, 0:NT * DV].rearrange("p (t e) -> p t e", t=NT)
                gagg_ready.wait(dve, s, i, n)
                nc.vector.reciprocal(rinv[s][:, h, :], agg[:, :, D]).then_inc(grinv[s], 1)
                grinv.wait(dve, s, i, n)
                nc.vector.tensor_tensor(
                    hn[s][:, :, h * D:(h + 1) * D], agg[:, :, 0:D],
                    rinv[s][:, h, :].unsqueeze(2).broadcast_to([P, NT, D]), ALU.mult).then_inc(gnorm[s], 1)

            with dve.Fori(0, STEPS) as i:
                norm_layer(i, 0)
                for s in streams:
                    valp_ready.wait(dve, s, i, 1)
                    nc.vector.tensor_copy(vals[s][:, :, 0:C], two_banks(s, 0)).then_inc(val_ready[s], 1)
                for t in range(NT):
                    for s in streams:
                        masked_max(i, s, 0, 0, t)
                    for s in streams:
                        masked.wait(dve, s, i, t + 1)
                        nc.vector.scalar_tensor_tensor(
                            out=prob[s][:, 0, t, :], in0=prob[s][:, 0, t, :], scalar=SLOPE,
                            in1=prob[s][:, 0, t, :], op0=ALU.mult, op1=ALU.max).then_inc(lrelu_ready[s], 1)
                for s in streams:
                    nc.vector.scalar_tensor_tensor(
                        out=negmax[s][:, 0, :], in0=rowmax[s][:, 0, :], scalar=SLOPE,
                        in1=rowmax[s][:, 0, :], op0=ALU.mult, op1=ALU.max).then_inc(shift_a[s], 1)
                for s in streams:
                    shift_a.wait(dve, s, i, 1)
                    nc.vector.tensor_scalar(negmax[s][:, 0, :], negmax[s][:, 0, :], -1.0, None,
                                            ALU.mult).then_inc(shift_ready[s], 1)
                for t in range(1, NT, 2):
                    for s in streams:
                        weights_out(i, s, 0, 0, t)
                for s in streams:
                    agg0_ready.wait(dve, s, i, 1)
                    nc.vector.reciprocal(rinv[s][:, 0, :], rowsum[s][:, 0, :]).then_inc(rinv0[s], 1)
                for s in streams:
                    rinv0.wait(dve, s, i, 1)
                    for t in range(NT):
                        last = nc.vector.tensor_scalar(hn[s][:, t, :], two_banks(s, 2)[:, t, :],
                                                       rinv[s][:, 0, t:t + 1], 0.0, ALU.mult, ALU.max)
                    last.then_inc(agg0_norm[s], 1)
                norm_layer(i, 1)
                gat(i, 1)
                norm_layer(i, 2)
                for s in streams:
                    qkp_ready.wait(dve, s, i, 1)
                    for k in range(KT):
                        last = nc.vector.tensor_scalar(kT[s][:, k, :], ps[s][:, 2 + k, :],
                                                       b_qk[:, 1, k:k + 1], None, ALU.add)
                    last.then_inc(kT_ready[s], 1)
                for s in streams:
                    valp_ready.wait(dve, s, i, 2)
                    nc.vector.tensor_tensor(vals[s][:, :, 0:C], two_banks(s, 0),
                                            b_rows[:, 0, :].unsqueeze(1).broadcast_to([P, NT, C]),
                                            ALU.add).then_inc(val_ready[s], 1)
                for h in range(-1, H):
                    if h + 1 < H:
                        for t in range(NT):
                            for s in streams:
                                masked_max(i, s, 2, h + 1, t)
                        for s in streams:
                            masked.wait(dve, s, i, att(2, h + 2, 0))
                            nc.vector.tensor_scalar(negmax[s][:, h + 1, :], rowmax[s][:, h + 1, :],
                                                    -QK_SCALE, None, ALU.mult).then_inc(shift_ready[s], 1)
                    if h >= 0:
                        for t in range(1, NT, 2):
                            for s in streams:
                                weights_out(i, s, 2, h, t)
                        for s in streams:
                            agg2_ready.wait(dve, s, i, h + 1)
                            nc.vector.reciprocal(rinv[s][:, h, :], rowsum[s][:, h, :]).then_inc(rinv2[s], 1)
                        for s in streams:
                            rinv2.wait(dve, s, i, h + 1)
                            nc.vector.tensor_tensor(
                                hn[s][:, :, h * D:(h + 1) * D],
                                ps[s][:, 3, 0:NT * D].rearrange("p (t d) -> p t d", t=NT),
                                rinv[s][:, h, :].unsqueeze(2).broadcast_to([P, NT, D]),
                                ALU.mult).then_inc(agg2_norm[s], 1)
                for s in streams:
                    wop_ready.wait(dve, s, i, 1)
                    nc.vector.tensor_tensor(hn[s][:, :, :], two_banks(s, 2),
                                            b_rows[:, 1, :].unsqueeze(1).broadcast_to([P, NT, C]),
                                            ALU.add).then_inc(o_ready[s], 1)
                    o_ready.wait(dve, s, i, 1)
                    statistics(i, s, "inner", hn[s])
                for s in streams:
                    mv_ready.wait(dve, s, i, NORMS["inner"] + 1)
                    for t in range(NT):
                        last = nc.vector.scalar_tensor_tensor(
                            out=hn[s][:, t, :], in0=hn[s][:, t, :], scalar=mv[s][:, t, 0:1],
                            in1=b_rows[:, 2, :], op0=ALU.subtract, op1=ALU.mult)
                    last.then_inc(on_ready[s], 1)
                for s in streams:
                    on_ready.wait(dve, s, i, 1)
                    xb_ready.wait(dve, s, i, 1)
                    rstd_ready.wait(dve, s, i, NORMS["inner"] + 1)
                    for t in range(NT):
                        last = nc.vector.scalar_tensor_tensor(
                            out=xc[s][:, t, :], in0=hn[s][:, t, :], scalar=rstd[s][:, t:t + 1],
                            in1=xc[s][:, t, :], op0=ALU.mult, op1=ALU.add)
                    last.then_inc(x2_ready[s], 1)
                    layer_statistics(i, s, 3)
                norm_layer(i, 3)
                gat(i, 3)

        @block.tensor
        def _(pe):
            pe.wait_ge(ident_ok, 3)
            pe.wait_ge(consts_in, CONSTS)
            for w in range(2):
                for k in range(KT):
                    for c in range(KT):
                        last = nc.tensor.transpose(ps[1][:, w * KT + k, c * P:(c + 1) * P],
                                                   w12[:, w, c, k * P:(k + 1) * P], ident[:, :])
            last.then_inc(setup_pe, 1)
            pe.wait_ge(masks_ok, 1)
            for j in range(NT):
                for t in range(NT):
                    last = nc.tensor.transpose(ps[0][:, j, t * P:(t + 1) * P],
                                               adj_pos[:, t, j * P:(j + 1) * P], ident[:, :])
            last.then_inc(setup_pe, 1)
            pe.wait_ge(setup_ok, 1)
            for c in range(KT):
                for k in range(KT):
                    last = nc.tensor.matmul(ps[1][:, c, 0:C], w12T[:, 0, k, c * P:(c + 1) * P],
                                            w12T[:, 1, k, :], start=(k == 0), stop=(k == KT - 1))
            last.then_inc(setup_pe, 1)
            pe.wait_ge(setup_ok, 2)
            pe.wait_ge(poison_ok, 2)
            nc.tensor.transpose(ps[0][0:1, 0, 0:P], part_any[:, 0:1], ident[:, :]).then_inc(setup_pe, 1)
            pe.wait_ge(setup_ok, 4)
            nc.tensor.transpose(ps[0][:, 1, 0:1], all_any[0:1, 0:1].broadcast_to([1, P]),
                                ident[0:1, 0:1]).then_inc(setup_pe, 1)
            pe.wait_ge(setup_ok, 5)

            def transposed(i, layer):
                for s in streams:
                    hn_ready.wait(pe, s, i, layer + 1)
                    for t in range(NT):
                        for k in range(KT):
                            last = nc.tensor.transpose(ps[s][:, k, t * P:(t + 1) * P],
                                                       hn[s][:, t, k * P:(k + 1) * P], ident[:, :])
                    last.then_inc(hTp_ready[s], 1)

            def to_rows(s, src, w, bank, width):
                for t in range(NT):
                    for k in range(KT):
                        last = nc.tensor.matmul(two_banks(s, bank)[:, t, :], src[s][:, k, t * P:(t + 1) * P],
                                                w[:, k, 0:width], start=(k == 0), stop=(k == KT - 1))
                return last

            def to_columns(s, w, bank):
                for m in range(KT):
                    for k in range(KT):
                        last = nc.tensor.matmul(ps[s][:, bank + m, :], w[:, k, m * P:(m + 1) * P],
                                                hT[s][:, k, :], start=(k == 0), stop=(k == KT - 1))
                return last

            def weights_transposed(i, s, layer, h, t):
                a = att(layer, h, t)
                bank = (2 + t) % 4 if layer == 0 else 2
                p_ready.wait(pe, s, i, a + 1)
                if layer == 2 and (h or t):
                    (pT_dve if t % 2 == 0 else pT_act).wait(pe, s, i, (a - 1) // 2 + 1)
                for j in range(NT):
                    last = nc.tensor.transpose(ps[s][:, bank, j * P:(j + 1) * P],
                                               prob[s][:, h % 2, t, j * P:(j + 1) * P], ident[:, :])
                last.then_inc(pTp_ready[s], 1)

            def gat(i, layer):
                g = GAT[layer]
                transposed(i, layer)
                for s in streams:
                    hT_ready.wait(pe, s, i, layer + 1)
                    for t in range(NT):
                        for k in range(KT):
                            last = nc.tensor.matmul(ps[s][:, t, 0:QE], hT[s][:, k, t * P:(t + 1) * P],
                                                    wgat[:, g, k, :], start=(k == 0), stop=(k == KT - 1))
                    last.then_inc(q_ready[s], 1)
                for s in streams:
                    qx_ready.wait(pe, s, i, g + 1)
                    for t in range(NT):
                        last = nc.tensor.transpose(ps[s][0:H, 0, t * P:(t + 1) * P], qx[s][:, t, C + H:QE],
                                                   ident[:, :])
                    last.then_inc(dT_ready[s], 1)
                for s in streams:
                    dmax_ready.wait_apart(pe, s, i, g + 1, pe_waits)
                    nc.tensor.transpose(ps[s][:, 1, 0:H], dmax[s][:, 0:1].broadcast_to([H, P]),
                                        ident[0:H, 0:H]).then_inc(dmax_bc[s], 1)
                for h in range(-1, H):
                    if h + 1 < H:
                        for s in streams:
                            if h < 0:
                                gval_ready.wait(pe, s, i, g + 1)
                            for t in range(NT):
                                last = nc.tensor.transpose(
                                    ps[s][:, 2 + (h + 1) % 2, t * P:(t + 1) * P],
                                    gval[s][:, 2, t, h + 1:h + 2].broadcast_to([P, P]), ident[:, :])
                            last.then_inc(r_ready[s], 1)
                    if h >= 0:
                        for s in streams:
                            if h == 0:
                                gvals_ready.wait(pe, s, i, g + 1)
                            gP_ready.wait(pe, s, i, g * H + h + 1)
                            for t in range(NT):
                                for j in range(NT):
                                    last = nc.tensor.matmul(
                                        ps[s][:, h % 2, t * DV:(t + 1) * DV],
                                        probT[s][:, h % 2, j, t * P:(t + 1) * P],
                                        vals[s][:, j, h * DV:(h + 1) * DV],
                                        start=(j == 0), stop=(j == NT - 1))
                            last.then_inc(gagg_ready[s], 1)

            with pe.Fori(0, STEPS) as i:
                transposed(i, 0)
                for s in streams:
                    hT_ready.wait(pe, s, i, 1)
                    to_columns(s, wA, 2).then_inc(uTp_ready[s], 1)
                for s in streams:
                    to_rows(s, hT, w3, 0, C).then_inc(valp_ready[s], 1)
                for t in range(NT):
                    for s in streams:
                        if t == 0:
                            uT_ready.wait(pe, s, i, 1)
                        if t == 2:
                            val_ready.wait(pe, s, i, 1)
                        for k in range(KT):
                            last = nc.tensor.matmul(ps[s][:, (2 + t) % 4, :], qT[s][:, k, t * P:(t + 1) * P],
                                                    hT[s][:, k, :], start=(k == 0), stop=(k == KT - 1))
                        last.then_inc(e_ready[s], 1)
                for t in range(NT + 1):
                    for s in streams:
                        if t < NT:
                            weights_transposed(i, s, 0, 0, t)
                    for s in streams:
                        if t:
                            u = t - 1
                            (pT_act if u % 2 == 0 else pT_dve).wait(pe, s, i, u // 2 + 1)
                            for j in range(NT):
                                last = nc.tensor.matmul(two_banks(s, 2)[:, u, :],
                                                        probT[s][:, 0, j, u * P:(u + 1) * P],
                                                        vals[s][:, j, 0:C], start=(j == 0), stop=(j == NT - 1))
                            if u == NT - 1:
                                last.then_inc(agg0_ready[s], 1)
                gat(i, 1)
                transposed(i, 2)
                for s in streams:
                    hT_ready.wait(pe, s, i, 3)
                    to_columns(s, wqkvo[:, 0, :, :], 0)
                    to_columns(s, wqkvo[:, 1, :, :], 2).then_inc(qkp_ready[s], 1)
                for s in streams:
                    qT_ready.wait(pe, s, i, 1)
                    to_rows(s, hT, wqkvo[:, 2, :, :], 0, C).then_inc(valp_ready[s], 1)
                for h in range(-1, H):
                    if h + 1 < H:
                        g = h + 1
                        at = slice((g % 2) * D, (g % 2 + 1) * D)
                        for t in range(NT):
                            for s in streams:
                                if g == 0 and t == 0:
                                    kT_ready.wait(pe, s, i, 1)
                                    val_ready.wait(pe, s, i, 2)
                                elif g or t >= 2:
                                    masked.wait(pe, s, i, att(2, g, t) - 1)
                                nc.tensor.matmul(ps[s][:, t % 2, :], qT[s][at, g // 2, t * P:(t + 1) * P],
                                                 kT[s][at, g // 2, :], start=True,
                                                 stop=True).then_inc(e_ready[s], 1)
                    if h >= 0:
                        for t in range(NT + 1):
                            for s in streams:
                                if t < NT:
                                    weights_transposed(i, s, 2, h, t)
                            for s in streams:
                                if t:
                                    u = t - 1
                                    a = att(2, h, u)
                                    (pT_act if u % 2 == 0 else pT_dve).wait(pe, s, i, a // 2 + 1)
                                    if u == 0 and h:
                                        agg2_norm.wait(pe, s, i, h)
                                    for j in range(NT):
                                        last = nc.tensor.matmul(
                                            ps[s][:, 3, u * D:(u + 1) * D],
                                            probT[s][:, 0, j, u * P:(u + 1) * P],
                                            vals[s][:, j, h * D:(h + 1) * D],
                                            start=(j == 0), stop=(j == NT - 1))
                                    if u == NT - 1:
                                        last.then_inc(agg2_ready[s], 1)
                for s in streams:
                    agg2_norm.wait(pe, s, i, H)
                    for t in range(NT):
                        for k in range(KT):
                            last = nc.tensor.transpose(ps[s][:, k, t * P:(t + 1) * P],
                                                       hn[s][:, t, k * P:(k + 1) * P], ident[:, :])
                    last.then_inc(oTp_ready[s], 1)
                for s in streams:
                    oT_ready.wait(pe, s, i, 1)
                    to_rows(s, qT, wqkvo[:, 3, :, :], 2, C).then_inc(wop_ready[s], 1)
                gat(i, 3)


_INS = ["x", "adj", "L0_gnn_W1", "L0_gnn_W2", "L0_gnn_W3", "L1_gnn_W", "L1_gnn_a", "L2_gnn_Wq",
        "L2_gnn_bq", "L2_gnn_Wk", "L2_gnn_bk", "L2_gnn_Wv", "L2_gnn_bv", "L2_gnn_Wo", "L2_gnn_bo",
        "L2_gnn_gamma", "L2_gnn_beta", "L3_gnn_W", "L3_gnn_a"]


def kernel(**inputs):
    import numpy as np
    import concourse.bacc as bacc
    from concourse.bass_utils import run_bass_kernel_spmd

    nc = bacc.Bacc("TRN2", target_bir_lowering=False, num_devices=1)
    arrays, args = {}, []
    for name in _INS:
        a = np.ascontiguousarray(inputs[name])
        arrays[f"in_{name}"] = a
        args.append(nc.dram_tensor(f"in_{name}", a.shape, mybir.dt.from_np(a.dtype),
                                   kind="ExternalInput").ap())
    out = nc.dram_tensor("out_x", inputs["x"].shape, mybir.dt.float32, kind="ExternalOutput").ap()
    gnn_stack_kernel(nc, *args, out)
    r = run_bass_kernel_spmd(nc, [arrays], core_ids=[0])
    return r.results[0]["out_x"]
```
